# Optimizing a Trainium2 kernel written in Bass

```python
import numpy as np
import jax
import jax.numpy as jnp

def _softmax(x, axis=-1):
    return jax.nn.softmax(x, axis=axis)

def _gelu(x):
    return jax.nn.gelu(x, approximate=True)

def _silu(x):
    return jax.nn.silu(x)

def _sigmoid(x):
    return jax.nn.sigmoid(x)

def _layernorm(x, axis=-1, eps=1e-05):
    m = jnp.mean(x, axis=axis, keepdims=True)
    v = jnp.var(x, axis=axis, keepdims=True)
    return (x - m) / jnp.sqrt(v + eps)

def _scatter_add(tgt, idx, src, axis=0):
    return tgt.at[idx].add(src)

def _segment_sum(src, seg, n):
    return jax.ops.segment_sum(src, seg, n)
kernel_name = 'mk_recurrent_d1_jaxref_r4_987214'

def setup_inputs(seed: int=0):
    np.random.seed(seed)
    _w = jnp.asarray

    def _L0_attn_setup():
        import jax, jax.numpy as jnp
        import numpy as np
        import math
        FACTOR = 1
        key = jax.random.key(seed)
        x = jax.random.normal(key, (8, 128, 1024), dtype=jnp.float32)
        return {'x': x}
    _L0_attn_in = _L0_attn_setup()

    def _L0_ffn_setup():
        import jax, jax.numpy as jnp
        import numpy as np
        LORA_SCALING = 1.0 / 2.0

        def _qlora_linear(x, wq, A, B):
            w = jnp.tile(wq, (1, 4))
            base = x @ w.T
            lora = x @ A.T @ B.T
            return base + lora * LORA_SCALING
        key = jax.random.key(seed)
        ks = jax.random.split(key, 10)
        d, h, r = (1024, 2752, 2)
        return {'x': jax.random.normal(ks[0], (16, 1, d), dtype=jnp.float32), 'w1q': jax.random.normal(ks[1], (h, d // 4), dtype=jnp.float32) * 0.02, 'a1': jax.random.normal(ks[2], (r, d), dtype=jnp.float32) * 0.02, 'b1': jax.random.normal(ks[3], (h, r), dtype=jnp.float32) * 0.02, 'w3q': jax.random.normal(ks[4], (h, d // 4), dtype=jnp.float32) * 0.02, 'a3': jax.random.normal(ks[5], (r, d), dtype=jnp.float32) * 0.02, 'b3': jax.random.normal(ks[6], (h, r), dtype=jnp.float32) * 0.02, 'w2q': jax.random.normal(ks[7], (d, h // 4), dtype=jnp.float32) * 0.02, 'a2': jax.random.normal(ks[8], (r, h), dtype=jnp.float32) * 0.02, 'b2': jax.random.normal(ks[9], (d, r), dtype=jnp.float32) * 0.02}
    _L0_ffn_in = _L0_ffn_setup()
    _d = {'L0_attn_x': _L0_attn_in['x'], 'L0_ffn_w1q': _L0_ffn_in['w1q'], 'L0_ffn_a1': _L0_ffn_in['a1'], 'L0_ffn_b1': _L0_ffn_in['b1'], 'L0_ffn_w3q': _L0_ffn_in['w3q'], 'L0_ffn_a3': _L0_ffn_in['a3'], 'L0_ffn_b3': _L0_ffn_in['b3'], 'L0_ffn_w2q': _L0_ffn_in['w2q'], 'L0_ffn_a2': _L0_ffn_in['a2'], 'L0_ffn_b2': _L0_ffn_in['b2']}
    _x0 = _d['L0_attn_x']
    _d['L0_attn_x'] = jax.random.normal(jax.random.fold_in(jax.random.key(seed), 1), (2, 2048, 1024), dtype=_x0.dtype)
    del _x0
    return _d

def reference(L0_attn_x, L0_ffn_w1q, L0_ffn_a1, L0_ffn_b1, L0_ffn_w3q, L0_ffn_a3, L0_ffn_b3, L0_ffn_w2q, L0_ffn_a2, L0_ffn_b2):

    def _L0_attn_ref(x):
        import jax, jax.numpy as jnp
        import numpy as np
        import math
        FACTOR = 1
        B, C, L = x.shape
        xh = x[:, None]
        f = jnp.fft.rfft(xh, axis=-1)
        corr = jnp.fft.irfft(f * jnp.conj(f), n=L, axis=-1)
        top_k = int(FACTOR * math.log(L))
        weights, delay = jax.lax.top_k(corr, top_k)
        tmp_corr = jax.nn.softmax(weights, axis=-1)
        init_index = jnp.arange(L)
        idx = (init_index[None, None, None, None, :] + delay[..., None]) % L
        pattern = jnp.take_along_axis(xh[:, :, :, None, :], idx, axis=-1)
        delays_agg = jnp.sum(pattern * tmp_corr[..., None], axis=-2)
        return delays_agg[:, 0]

    def _L0_ffn_ref(x, w1q, a1, b1, w3q, a3, b3, w2q, a2, b2):
        import jax, jax.numpy as jnp
        import numpy as np
        LORA_SCALING = 1.0 / 2.0

        def _qlora_linear(x, wq, A, B):
            w = jnp.tile(wq, (1, 4))
            base = x @ w.T
            lora = x @ A.T @ B.T
            return base + lora * LORA_SCALING
        gate = jax.nn.silu(_qlora_linear(x, w1q, a1, b1))
        up = _qlora_linear(x, w3q, a3, b3)
        return _qlora_linear(gate * up, w2q, a2, b2)
    x = L0_attn_x
    xn = _layernorm(x, axis=-1)
    s = _L0_attn_ref(xn)
    g = _silu(_L0_ffn_ref(xn, L0_ffn_w1q, L0_ffn_a1, L0_ffn_b1, L0_ffn_w3q, L0_ffn_a3, L0_ffn_b3, L0_ffn_w2q, L0_ffn_a2, L0_ffn_b2))
    x = x + s * g
    return x

_drawn_inputs = setup_inputs


def setup_inputs(seed=0):
    import zlib

    import numpy as np

    out = dict(_drawn_inputs(seed))
    spreads = {}
    factors = {'L0_ffn_a1': 8.0,
     'L0_ffn_b1': 8.0,
     'L0_ffn_a3': 8.0,
     'L0_ffn_b3': 8.0,
     'L0_ffn_a2': 8.0,
     'L0_ffn_b2': 8.0}
    for name, (base, spread) in spreads.items():
        noise = np.random.default_rng([zlib.crc32(name.encode()), seed]).standard_normal(out[name].shape)
        drawn = base * np.exp(spread * noise) if base else spread * noise
        out[name] = jnp.asarray(drawn.astype(out[name].dtype))
    for name, factor in factors.items():
        out[name] = (out[name] * factor).astype(out[name].dtype)
    return out
```

```python
import numpy as np
from contextlib import ExitStack

import concourse.bass as bass
from concourse import mybir

F32, F32R, F16 = mybir.dt.float32, mybir.dt.float32r, mybir.dt.float16
BF16, I32, U32 = mybir.dt.bfloat16, mybir.dt.int32, mybir.dt.uint32
ACT = mybir.ActivationFunctionType
ALU = mybir.AluOpType
AX_X = mybir.AxisListType.X
RMAX = bass.bass_isa.ReduceOp.max
RADD = bass.bass_isa.ReduceOp.add

P = 128
L = 1024
TOK = 4096
G = 512
NG = TOK // G
NQ = G // P
HID = 2752
HQ = HID // 4
HN = HQ // P
TAIL = HQ - HN * P
NP_ = 4 * HN + 2
W2 = 2 * TAIL
DQ = L // 4
EPS = 1e-5
TOPK = 6
NSLOT = NP_ + 4 + 4
NUSE = 15
USE_T, USE_XFT, USE_XA = 4, 12, 14
N_CONST = 6
T_AT = (9, 13, 17, 20)
STATS_AT = (0, 4, 11, 15)
NORM_AT = (1, 6, 12, 16)
INV_AT = (1, 3, 5, 7)


def pair_rows(p):
    return P if p < 4 * HN else W2


def pair_col(p):
    return p * P if p < 4 * HN else 4 * HN * P + (p - 4 * HN) * W2


def hidden_order():
    o = [j * HQ + n * P + np.arange(P) for n in range(HN) for j in range(4)]
    o += [j * HQ + HN * P + np.arange(TAIL) for j in range(4)]
    return np.concatenate(o)


def constants():
    w = 2 * np.pi / L
    even_a = np.concatenate([[256], np.arange(2, 256, 2)])
    even_b = np.concatenate([[-1], 512 - np.arange(2, 256, 2)])
    odd_a = np.arange(1, 256, 2)
    odd_b = 512 - odd_a
    ev, od = np.concatenate([even_a, even_b]), np.concatenate([odd_a, odd_b])

    def table(fn, t, f):
        m = fn(w * ((t[:, None] * f[None, :]) % L))
        m[:, f < 0] = 0
        m[np.abs(m) < 1e-12] = 0
        return m

    t0, t1 = np.arange(256), np.arange(1, 257)
    se = table(np.sin, t1, ev)
    se[255] = 0
    fwd = np.stack([table(np.cos, t0, ev), table(np.cos, t0, od), table(np.sin, t1, od), se])
    fwd = fwd.reshape(8, P, 256).transpose(1, 0, 2)
    mid = np.zeros((P, 256))
    mid[127] = table(np.cos, np.array([256]), ev)[0]
    tau_e, tau_o = np.arange(2, 513, 2), np.arange(1, 512, 2)
    inv = np.stack([table(np.cos, even_a, tau_e), table(np.cos, odd_a, tau_e),
                    table(np.cos, even_a, tau_o), table(np.cos, odd_a, tau_o)], 1)

    def halves(m):
        hi = m.astype(np.float16)
        return hi, (m - hi.astype(np.float64)).astype(np.float16)

    low = np.zeros((P, 4), np.float32)
    for q in range(4):
        low[32 * q + 8:32 * q + 12, 0] = low[32 * q + 20:32 * q + 24, 0] = -1
        low[32 * q + 4:32 * q + 8, 1] = low[32 * q + 16:32 * q + 20, 1] = -1
    low[4:6, 2] = low[10:12, 2] = -1
    low[98:100, 3] = low[104:106, 3] = -1
    (fh, fl), (ih, il) = halves(fwd), halves(inv)
    return dict(fwd_h=fh, fwd_l=fl, mid=mid.astype(np.float16), inv_h=ih, inv_l=il, low=low,
                ident=np.eye(P, dtype=np.float32))


def build(nc, d):
    x_d = d["x"].rearrange("(n p) c -> n p c", p=P)
    out_d = d["out"].rearrange("(n p) c -> n p c", p=P)

    with ExitStack() as ctx:
        place = [1152]

        def sb(name, shape, dt, at=None):
            size = int(np.prod(shape[1:])) * (2 if dt in (F16, BF16) else 4)
            offset = place[0] if at is None else at
            if at is None:
                place[0] += (size + 31) // 32 * 32
            return nc.alloc_sbuf_tensor_at(name, shape, dt, offset=offset)

        def sem(name):
            return ctx.enter_context(nc.semaphore(name))

        wt_h = [sb(f"w{m}_h", [P, 2, HID], F16) for m in (1, 3)]
        wt_l = [sb(f"w{m}_l", [P, 2, HID], F16) for m in (1, 3)]
        w2_h = sb("w2_h", [P, HN + 1, L], F32R)
        w2_l = sb("w2_l", [P, HN + 1, L], F32R)
        bst = sb("bst", [P, 6, 2, P], F32R)
        a2st = sb("a2st", [P, NP_, 12], F32R)
        ast = sb("ast", [P, 8, P], BF16)
        fwd_h = sb("fwd_h", [P, 8, 256], F16)
        fwd_l = sb("fwd_l", [P, 8, 256], F16)
        mid = sb("mid", [P, 256], F16)
        inv_h = sb("inv_h", [P, 4, 256], F16)
        inv_l = sb("inv_l", [P, 4, 256], F16)
        ident = sb("ident", [P, P], F32)
        low = sb("low", [P, 4], F32)
        xfs = [sb(f"xf{b}", [P, L], F32) for b in range(2)]
        xn = sb("xn", [P, L], F32)
        mir = sb("mir", [P, L], F32)
        xq = sb("xq", [P, NQ, DQ], F32)
        ft_h = sb("ft_h", [P, 8, G], F16)
        ft_l = sb("ft_l", [P, 8, G], F16)
        xt_h = sb("xt_h", [P, 2, G], F16)
        xt_l = sb("xt_l", [P, 2, G], F16)
        z_at = place[0]
        zst = [sb(f"zst{q}", [P, G], F32R) for q in range(4)]
        z_hi = sb("z_hi", [P, G], F32R)
        hf_at = place[0]
        hf_h = sb("hf_h", [P, HN + 1, G], F32R)
        hf_l = sb("hf_l", [P, HN + 1, G], F32R)
        qt_h = sb("qt_h", [P, 4, G], F16, at=hf_at + 3 * 4 * G)
        qt_l = sb("qt_l", [P, 4, G], F16, at=hf_at + (HN + 1 + 3) * 4 * G)
        hh_at = place[0]
        hh = sb("hh", [P, 2, G], F32R)
        hl = sb("hl", [P, 2, G], F32R)
        work_at = place[0]
        h_at = work_at
        h = sb("h", [P, 2, G], F32)
        sil = sb("sil", [P, 2, G], F32)
        acc = sb("acc", [P, 2, G], F32)
        sq_at = place[0]
        sq = sb("sq", [P, 2, G], F32)
        pa = sb("pa", [P, G], F32)
        pb = sb("pb", [P, G], F32)
        qp = sb("qp", [P, G], F32)
        corr = sb("corr", [P, L], F32, at=sq_at)
        z2f = pa[0:12, :]
        wmax = sb("wmax", [P, 2, 2], F32)
        wall = sb("wall", [P, 2], F32)
        wone = sb("wone", [P, 2], F32)
        wpow = sb("wpow", [P, 2], I32)
        winv = sb("winv", [P, 2], F32)
        wscl = sb("wscl", [P, 2], F32)
        bscl = sb("bscl", [P, 2], F32)
        bn = sb("bn", [P, 12], F32)
        mv = sb("mv", [P, 4, 2], F32)
        ve = sb("ve", [P, 4], F32)
        three = sb("three", [P, 3], F32)
        rs = sb("rs", [P, 4], F32)
        nm = sb("nm", [P, 4], F32)
        xsum = sb("xsum", [P, 4, 2], F32)
        c_rs = sb("c_rs", [P, 4], F32)
        c_nm = sb("c_nm", [P, 4], F32)
        c_0 = sb("c_0", [P, 4], F32)
        c_sq = sb("c_sq", [P, 4, 2], F32)
        c_b = sb("c_b", [P, 2, 4], F32)
        c_t = sb("c_t", [P, 4], F32)
        c_u = sb("c_u", [P, 4], F32)
        v8 = sb("v8", [P, 4, 8], F32)
        i8 = sb("i8", [P, 4, 8], U32)
        dv = sb("dv", [P, 4, 8], F32)
        ex = sb("ex", [P, 4, TOPK], F32)
        den = sb("den", [P, 4], F32)
        wts = sb("wts", [P, 4, 8], F32)
        rest = sb("rest", [P, 1], F32)
        rest2 = sb("rest2", [P, 1], F32)
        rest_all = sb("rest_all", [P, 1], F32)
        some = sb("some", [P, 1], I32)
        delay = sb("delay", [P, 8], I32)
        dtmp = sb("dtmp", [P, 8], I32)
        bit_i = sb("bit_i", [P, 10], I32)
        bit = sb("bit", [P, 10], F32)
        nbit = sb("nbit", [P, 10], F32)
        wk = sb("wk", [P, 8], F32)
        wtmp = sb("wtmp", [P, 8], F32)
        assert place[0] <= nc.sbuf_usable_end, place[0]
        xqf = xq[:].rearrange("p q c -> p (q c)")
        raw_w = [sb("raw_w1", [P, 2, HID], F32, at=hf_at), sb("raw_w3", [P, 2, HID], F32, at=work_at)]
        raw_w2 = sb("raw_w2", [P, HN + 1, L], F32, at=hf_at)
        raw_b = sb("raw_b", [P, 6, 2, P], F32, at=z_at)
        b_hi = sb("b_hi", [P, 6, 2, P], F32R, at=hh_at)
        raw_a2 = sb("raw_a2", [P, NP_, 2], F32, at=hh_at + 6144)
        a2_h = sb("a2_h", [P, NP_, 2], F32R, at=hh_at + 6144 + 192)
        a2_l = sb("a2_l", [P, NP_, 2], F32R, at=hh_at + 6144 + 384)
        a_bf = sb("a_bf", [P, 3, 32], BF16, at=hh_at + 6144 + 576)
        a_r = sb("a_r", [P, 2, 32], F32, at=hh_at + 6144 + 768)
        zh2 = sb("zh2", [12, G], F32R, at=h_at + 4 * 2 * G)
        rot = [sb("rot0", [P, L], F32, at=h_at + 4 * L), sb("rot1", [P, L], F32, at=h_at + 8 * L)]
        agg = sb("agg", [P, L], F32, at=h_at)

        def psum(name, shape, dt=F32):
            return ctx.enter_context(nc.psum_tensor(name, shape, dt))

        gb = [psum(f"g{i}", [P, 512]) for i in range(2)]
        ub = [psum(f"u{i}", [P, 512]) for i in range(2)]
        zb = psum("zb", [P, 512])
        mb = [psum(f"m{i}", [P, 512]) for i in range(3)]

        c_loaded = sem("c_loaded")
        w_loaded = [sem("w1_loaded"), sem("w3_loaded")]
        w2_loaded, x_loaded = sem("w2_loaded"), [sem("x0_loaded"), sem("x1_loaded")]
        a_loaded, stored = sem("a_loaded"), sem("stored")
        xr_loaded = [sem("xr0_loaded"), sem("xr1_loaded")]
        wmax_done, wall_done, wscl_done = sem("wmax_done"), sem("wall_done"), sem("wscl_done")
        wh_done, wl_done = sem("wh_done"), sem("wl_done")
        w2h_done, w2l_done = sem("w2h_done"), sem("w2l_done")
        a2h_done, b_hi_done, b_sc_done = sem("a2h_done"), sem("b_hi_done"), sem("b_sc_done")
        small_done, zeroed = sem("small_done"), sem("zeroed")
        stats_done, dev_done, normed, mirrored = sem("stats_done"), sem("dev_done"), sem("normed"), sem("mirrored")
        quartered = sem("quartered")
        folded, m_ready, m_hi, m_free = sem("folded"), sem("m_ready"), sem("m_hi"), sem("m_free")
        inv_read, z_done = sem("inv_read"), sem("z_done")
        g_ready, u_ready, sil_done, mult_done = sem("g_ready"), sem("u_ready"), sem("sil_done"), sem("mult_done")
        hh_done, hl_done, z2_done, acc_done = sem("hh_done"), sem("hl_done"), sem("z2_done"), sem("acc_done")
        hfh_done, hfl_done = sem("hfh_done"), sem("hfl_done")
        zh2_done, z2_read = sem("zh2_done"), sem("z2_read")
        dn_read, s_done, final_done = sem("dn_read"), sem("s_done"), sem("final_done")
        sq_done, p_done, q_done, qh_done, ql_done = (sem("sq_done"), sem("p_done"), sem("q_done"),
                                                     sem("qh_done"), sem("ql_done"))
        cur_done, top_done, dv_done, ex_done = sem("cur_done"), sem("top_done"), sem("dv_done"), sem("ex_done")
        rest_done, rall_done = sem("rest_done"), sem("rall_done")

        def at_slot(i, s):
            return i * NSLOT + s + 5
        def at_use(i, k):
            return i * NUSE + k + 13
        def at_free(i, k):
            return i * 11 + k + 9
        def at_high(i, k):
            return i * 11 + k + 8
        def at_pair(i, p):
            return i * NP_ + p + 1
        def at_tile(i, q, per=1, n=1):
            return i * 4 * per + q * per + n


        block = ctx.enter_context(nc.Block())

        @block.sync
        def _(sp):
            def front_load(i, q):
                sp.dma_start(xfs[q % 2][:], x_d[(i + 1) * 4 + q]).then_inc(x_loaded[q % 2], 16)

            def again_load(i, q):
                sp.dma_start(xfs[q % 2][:], x_d[i * 4 + q]).then_inc(xr_loaded[q % 2], 16)

            def body(i, last):
                sp.wait_ge(m_ready, at_use(i - 1, USE_T + 7))
                sp.wait_ge(stored, (i * 4 + 1) * 16)
                if not last:
                    front_load(i, 0)
                    front_load(i, 1)
                    for q in range(2):
                        sp.wait_ge(m_ready, at_use(i, USE_T + 2 * q + 1))
                        front_load(i, q + 2)
                for q in range(2):
                    if not last:
                        sp.wait_ge(m_ready, at_use(i, USE_T + 2 * q + 5))
                    again_load(i, q)
                for q in range(4):
                    sp.wait_ge(final_done, at_tile(i, q))
                    sp.dma_start(out_d[i * 4 + q], xfs[q % 2][:]).then_inc(stored, 16)
                    if q < 2:
                        sp.wait_ge(stored, (i * 4 + q + 2) * 16)
                        again_load(i, q + 2)

            front_load(-1, 0)
            sp.dma_start(xn[0:4, :], d["a13"]).then_inc(a_loaded, 16)
            sp.dma_start(ident[:], d["ident"]).then_inc(a_loaded, 16)
            front_load(-1, 1)
            sp.dma_start(raw_w[0][:], d["w1t"]).then_inc(w_loaded[0], 16)
            sp.dma_start(low[:], d["low"]).then_inc(stored, 16)
            sp.dma_start(raw_b[:], d["b13"]).then_inc(w_loaded[1], 16)
            sp.dma_start(raw_w[1][:], d["w3t"]).then_inc(w_loaded[1], 16)
            for q in range(2):
                sp.wait_ge(m_ready, at_use(-1, USE_T + 2 * q + 1))
                front_load(-1, q + 2)
                if q == 0:
                    for sbuf, name in ((raw_a2, "a2t"), (fwd_h, "fwd_h"), (fwd_l, "fwd_l"), (mid, "mid"),
                                       (inv_h, "inv_h"), (inv_l, "inv_l")):
                        sp.dma_start(sbuf[:], d[name]).then_inc(c_loaded, 16)
            sp.wait_ge(wl_done, 2)
            sp.dma_start(raw_w2[:], d["w2t"]).then_inc(w2_loaded, 16)
            with sp.Fori(0, NG - 1) as i:
                body(i, False)
            body(NG - 1, True)
            sp.wait_ge(stored, (TOK // P + 1) * 16)

        @block.gpsimd
        def _(pool):
            tt = nc.gpsimd.tensor_tensor

            def mirror(m, r):
                tt(m[:, 1:512], r[:, 1:512], r[:, 1023:512:-1], ALU.add).then_inc(mirrored, 1)
                nc.gpsimd.tensor_copy(m[:, 0:513:512], r[:, 0:513:512]).then_inc(mirrored, 1)
                tt(m[:, 513:1024], r[:, 1:512], r[:, 1023:512:-1], ALU.subtract).then_inc(mirrored, 1)

            def mirror_again(f, m):
                tt(f[:, 0:256], m[:, 0:256], m[:, 512:256:-1], ALU.add)
                tt(f[:, 256:512], m[:, 0:256], m[:, 512:256:-1], ALU.subtract)
                tt(f[:, 512:767], m[:, 513:768], m[:, 1023:768:-1], ALU.add)
                tt(f[:, 768:1023], m[:, 513:768], m[:, 1023:768:-1], ALU.subtract)
                nc.gpsimd.tensor_copy(f[:, 767:1024:256], m[:, 768:255:-512]).then_inc(folded, 1)

            def front(i, q):
                tile = (i + 1) * 4 + q
                pool.wait_ge(stats_done, tile + 1)
                tt(ve[:, q:q + 1], mv[:, q, 1:2], three[:, 0:1], ALU.add).then_inc(dev_done, 1)
                tt(nm[:, q:q + 1], mv[:, q, 0:1], three[:, 2:3], ALU.mult)
                pool.wait_ge(dev_done, 3 * tile + 1)
                tt(rs[:, q:q + 1], ve[:, q:q + 1], three[:, 1:2], ALU.pow).then_inc(dev_done, 1)
                pool.wait_ge(dev_done, 3 * tile + 2)
                tt(nm[:, q:q + 1], nm[:, q:q + 1], rs[:, q:q + 1], ALU.mult).then_inc(dev_done, 1)
                pool.wait_ge(normed, (tile + 1) * 2)
                mirror(mir, xn)
                pool.wait_ge(mirrored, tile * 3 + 6)
                mirror_again(xfs[q % 2], mir)
                quarters = xq[:, q, :]
                tt(quarters, xn[:, 0:256], xn[:, 256:512], ALU.add).then_inc(quartered, 1)
                pool.wait_ge(quartered, tile * 3 + 1)
                tt(quarters, quarters, xn[:, 512:768], ALU.add).then_inc(quartered, 1)
                pool.wait_ge(quartered, tile * 3 + 2)
                tt(quarters, quarters, xn[:, 768:1024], ALU.add).then_inc(quartered, 1)

            def body(i, last):
                if not last:
                    for q in range(4):
                        front(i, q)
                pool.wait_ge(rest_done, i + 1)
                tt(rest2[:], rest[:], rest[:], ALU.add)
                nc.gpsimd.drain()
                nc.gpsimd.partition_all_reduce(rest_all[:], rest2[:], P, RADD).then_inc(rall_done, 1)

            nc.gpsimd.memset(ast[:], 0.0).then_inc(zeroed, 1)
            for n, value in enumerate((EPS, -0.5, -1.0)):
                nc.gpsimd.memset(three[:, n:n + 1], value).then_inc(zeroed, 1)
            pool.wait_ge(zeroed, 4)
            pool.wait_ge(a_loaded, 32)
            mirror(mir[0:4, :], xn[0:4, :])
            pool.wait_ge(mirrored, 3)
            mirror_again(xqf[0:4, :], mir[0:4, :])

            def largest(m):
                pool.wait_ge(wmax_done, m + 1)
                nc.gpsimd.partition_all_reduce(wall[:, m:m + 1], wone[:, m:m + 1], P, RMAX).then_inc(wall_done, 1)

            pool.wait_ge(m_ready, 1)
            front(-1, 0)
            largest(0)
            front(-1, 1)
            front(-1, 2)
            largest(1)
            front(-1, 3)
            with pool.Fori(0, NG - 1) as i:
                body(i, False)
            body(NG - 1, True)

        @block.scalar
        def _(act):
            def A(out, in_, f=ACT.Identity, **kw):
                return nc.scalar.activation(out, in_, f, **kw)

            def normalise(i, q):
                tile = (i + 1) * 4 + q
                act.wait_ge(dev_done, 3 * tile + 3)
                for half in range(2):
                    A(xn[:, half::2], xfs[q % 2][:, half::2], scale=rs[:, q:q + 1], bias=nm[:, q:q + 1],
                      accum_out=xsum[:, q, half:half + 1]).then_inc(normed, 1)

            def folds_high(i, q):
                for k in range(2):
                    use = USE_T + 2 * q + k
                    act.wait_ge(m_ready, at_use(i, use))
                    A(ft_h[:, 4 * k:4 * k + 4, q * P:(q + 1) * P],
                      mb[use % 3][:].rearrange("p (k t) -> p k t", k=4), ACT.Copy).then_inc(m_hi, 1)

            def quarters_high(i):
                for k in range(2):
                    act.wait_ge(m_ready, at_use(i, USE_XFT + k))
                    A(xt_h[:, k, :], mb[(USE_XFT + k) % 3][:], ACT.Copy).then_inc(m_hi, 1)

            def z_high(i):
                act.wait_ge(m_ready, at_use(i, USE_XA))
                A(z_hi[:], mb[USE_XA % 3][:], ACT.Copy).then_inc(m_hi, 1)

            def squares(i):
                for dd in range(4):
                    b = (NP_ + 4 + dd) % 2
                    if dd:
                        act.wait_ge(p_done, at_tile(i + 1, dd - 1))
                    act.wait_ge(g_ready, at_slot(i, NP_ + 4 + dd))
                    A(sq[:, 0, :], gb[b][:], ACT.Square, scale=0.25).then_inc(sq_done, 1)
                    act.wait_ge(u_ready, at_slot(i, NP_ + 4 + dd))
                    A(sq[:, 1, :], ub[b][:], ACT.Square, scale=0.25).then_inc(sq_done, 1)
                    if dd % 2:
                        e = dd // 2
                        for sign, buf in enumerate((qp, pb)):
                            act.wait_ge(q_done, at_tile(i + 1, 2 * e + sign))
                            A(qt_h[:, 2 * sign + e, :], buf[:], ACT.Copy).then_inc(qh_done, 1)

            def inverse_read(i, q):
                act.wait_ge(m_ready, at_use(i, q))
                if q == 0:
                    act.wait_ge(cur_done, i + 1)
                else:
                    act.wait_ge(top_done, at_tile(i, q - 1))
                m = mb[q % 3]
                be, bo = c_b[:, 0, q:q + 1], c_b[:, 1, q:q + 1]
                A(corr[:, 0:1], c_0[:, q:q + 1], ACT.Copy)
                A(corr[:, 2:513:2], m[:, 0:256], scale=1 / 32, bias=be)
                A(corr[:, 1022:512:-2], m[:, 0:255], scale=1 / 32, bias=be)
                A(corr[:, 1:512:2], m[:, 256:512], scale=1 / 32, bias=bo)
                A(corr[:, 1023:512:-2], m[:, 256:512], scale=1 / 32, bias=bo).then_inc(inv_read, 1)

            def gate(i, p):
                n = pair_rows(p)
                act.wait_ge(g_ready, at_slot(i, p))
                if p >= 2:
                    act.wait_ge(mult_done, at_pair(i, p - 2))
                A(sil[0:n, p % 2, :], gb[p % 2][0:n, :], ACT.Silu, scale=winv[0:n, 0:1]).then_inc(sil_done, 1)

            def hidden_high(i, p):
                n = pair_rows(p)
                if p >= 2:
                    act.wait_ge(z2_done, at_pair(i, p - 2))
                act.wait_ge(mult_done, at_pair(i, p))
                A(hh[0:n, p % 2, :], h[0:n, p % 2, :], ACT.Copy).then_inc(hh_done, 1)

            def folded_high(i, n):
                rows = P if n < HN else W2
                act.wait_ge(acc_done, at_pair(i, min(4 * n + 3, NP_ - 1)))
                A(hf_h[0:rows, n, :], acc[0:rows, n % 2, :], ACT.Copy).then_inc(hfh_done, 1)

            def down(i):
                for q in range(4):
                    s = NP_ + q
                    buf = xfs[q % 2]
                    act.wait_ge(xr_loaded[q % 2], (i * 2 + q // 2 + 1) * 16)
                    if q:
                        act.wait_ge(final_done, at_tile(i, q - 1))
                    A(xn[:], buf[:], scale=c_rs[:, q:q + 1], bias=c_nm[:, q:q + 1]).then_inc(s_done, 1)
                    act.wait_ge(g_ready, at_slot(i, s))
                    A(mir[:, 0:512], gb[s % 2][:], ACT.Silu).then_inc(dn_read, 1)
                    act.wait_ge(u_ready, at_slot(i, s))
                    A(mir[:, 512:1024], ub[s % 2][:], ACT.Silu).then_inc(dn_read, 1)

            def body(i, last):
                for p in range(NP_):
                    gate(i, p)
                    if p:
                        hidden_high(i, p - 1)
                    if p - 1 in INV_AT:
                        inverse_read(i, INV_AT.index(p - 1))
                    if p == 12:
                        act.wait_ge(dv_done, i + 1)
                        A(ex[:], dv[:, :, 0:TOPK], ACT.Exp).then_inc(ex_done, 1)
                    if not last and p in NORM_AT:
                        normalise(i, NORM_AT.index(p))
                    if not last and p - 1 in T_AT:
                        folds_high(i, T_AT.index(p - 1))
                    if p % 4 == 1 and p > 1:
                        folded_high(i, p // 4 - 1)
                hidden_high(i, NP_ - 1)
                if not last:
                    quarters_high(i)
                folded_high(i, HN)
                act.wait_ge(z2_done, at_pair(i, NP_ - 1))
                A(zh2[:], zb[0:12, :], ACT.Copy, scale=0.5).then_inc(zh2_done, 1)
                if not last:
                    z_high(i)
                down(i)
                if not last:
                    squares(i)

            def w_high(m):
                act.wait_ge(wscl_done, m + 1)
                for k in range(2):
                    A(wt_h[m][:, k, :], raw_w[m][:, k, :], scale=wscl[:, m:m + 1]).then_inc(wh_done, 1)

            normalise(-1, 0)
            normalise(-1, 1)
            folds_high(-1, 0)
            w_high(0)
            normalise(-1, 2)
            folds_high(-1, 1)
            normalise(-1, 3)
            w_high(1)
            act.wait_ge(b_sc_done, 1)
            A(b_hi[:], raw_b[:], ACT.Copy).then_inc(b_hi_done, 1)
            act.wait_ge(c_loaded, 16 * N_CONST)
            A(a2_h[:], raw_a2[:], ACT.Copy).then_inc(a2h_done, 1)
            folds_high(-1, 2)
            folds_high(-1, 3)
            quarters_high(-1)
            z_high(-1)
            act.wait_ge(w2_loaded, 16)
            for n in range(HN + 1):
                A(w2_h[:, n, :], raw_w2[:, n, :], ACT.Copy).then_inc(w2h_done, 1)
            act.wait_ge(wl_done, 4)
            squares(-1)
            with act.Fori(0, NG - 1) as i:
                body(i, False)
            body(NG - 1, True)

        @block.vector
        def _(dve):
            tt, ts, stt = nc.vector.tensor_tensor, nc.vector.tensor_scalar, nc.vector.scalar_tensor_tensor

            def stats(i, q):
                tile = (i + 1) * 4 + q
                dve.wait_ge(x_loaded[q % 2], ((i + 1) * 2 + q // 2 + 1) * 16)
                nc.vector.bn_stats(bn[:, 0:6], xfs[q % 2][:, 0:512])
                nc.vector.bn_stats(bn[:, 6:12], xfs[q % 2][:, 512:1024])
                nc.vector.drain()
                nc.vector.bn_aggr(mv[:, q, :], bn[:]).then_inc(stats_done, 1)

            def current(i):
                dve.wait_ge(normed, (i + 1) * 8)
                nc.vector.tensor_copy(c_rs[:], rs[:])
                nc.vector.tensor_copy(c_nm[:], nm[:])
                stt(out=c_t[:], in0=mv[:, :, 1], scalar=float(L), in1=rs[:], op0=ALU.mult, op1=ALU.mult)
                tt(c_sq[:], xsum[:], xsum[:], ALU.mult)
                stt(out=c_b[:, 1, :], in0=xsum[:, :, 0], scalar=4.0 / L, in1=xsum[:, :, 1],
                    op0=ALU.mult, op1=ALU.mult)
                nc.vector.drain()
                tt(c_0[:], c_t[:], rs[:], ALU.mult)
                tt(c_u[:], c_sq[:, :, 0], c_sq[:, :, 1], ALU.add)
                nc.vector.drain()
                ts(c_b[:, 0, :], c_u[:], 2.0 / L, None, ALU.mult).then_inc(cur_done, 1)

            def folds_low(i, q):
                for k in range(2):
                    use = USE_T + 2 * q + k
                    dve.wait_ge(m_hi, at_high(i, use))
                    hi = ft_h[:, 4 * k:4 * k + 4, q * P:(q + 1) * P]
                    tt(ft_l[:, 4 * k:4 * k + 4, q * P:(q + 1) * P],
                       mb[use % 3][:].rearrange("p (k t) -> p k t", k=4), hi, ALU.subtract).then_inc(m_free, 1)

            def quarters_low(i):
                for k in range(2):
                    dve.wait_ge(m_hi, at_high(i, USE_XFT + k))
                    tt(xt_l[:, k, :], mb[(USE_XFT + k) % 3][:], xt_h[:, k, :], ALU.subtract).then_inc(m_free, 1)

            def z_stack(i):
                dve.wait_ge(m_hi, at_high(i, USE_XA))
                for q in range(4):
                    r = slice(32 * q, 32 * q + 32)
                    o = stt(out=zst[q][r, :], in0=z_hi[r, :].bitcast(F32), scalar=low[r, 0:1],
                            in1=mb[USE_XA % 3][r, :], op0=ALU.mult, op1=ALU.add)
                o.then_inc(m_free, 1)

            def spectrum(i):
                for dd in range(4):
                    e = dd // 2
                    dve.wait_ge(sq_done, at_tile(i + 1, dd, 2, 2))
                    tt((pb if dd % 2 else pa)[:], sq[:, 0, :], sq[:, 1, :], ALU.add).then_inc(p_done, 1)
                    if dd % 2:
                        dve.wait_ge(p_done, at_tile(i + 1, dd))
                        tt(qp[:], pa[:], pb[:], ALU.add).then_inc(q_done, 1)
                        tt(pb[:], pa[:], pb[:], ALU.subtract).then_inc(q_done, 1)
                        for sign, buf in enumerate((qp, pb)):
                            dve.wait_ge(qh_done, at_tile(i + 1, 2 * e + sign))
                            tt(qt_l[:, 2 * sign + e, :], buf[:], qt_h[:, 2 * sign + e, :],
                               ALU.subtract).then_inc(ql_done, 1)

            def top(i, q):
                dve.wait_ge(inv_read, at_tile(i, q))
                nc.vector.tensor_copy(dv[:, q, 6:7], corr[:, 0:1])
                nc.vector.max(v8[:, q, :], corr[:])
                nc.vector.drain()
                nc.vector.max_index(i8[:, q, :], v8[:, q, :], corr[:]).then_inc(top_done, 1)

            def distances():
                for q in range(4):
                    o = ts(dv[:, q, 0:TOPK], v8[:, q, 0:TOPK], v8[:, q, 0:1], None, ALU.subtract)
                o.then_inc(dv_done, 1)

            def weights(i):
                dve.wait_ge(ex_done, i + 1)
                nc.vector.tensor_reduce(rest[:], ex[:, :, 1:TOPK], mybir.AxisListType.XY, ALU.add).then_inc(rest_done, 1)
                nc.vector.tensor_reduce(den[:], ex[:], AX_X, ALU.add)
                nc.vector.drain()
                nc.vector.reciprocal(den[:], den[:])
                nc.vector.drain()
                for q in range(4):
                    ts(wts[:, q, 0:TOPK], ex[:, q, :], den[:, q:q + 1], None, ALU.mult)

            def product(i, p):
                n = pair_rows(p)
                dve.wait_ge(sil_done, at_pair(i, p))
                if p >= 2:
                    dve.wait_ge(acc_done, at_pair(i, p - 2))
                dve.wait_ge(u_ready, at_slot(i, p))
                stt(out=h[0:n, p % 2, :], in0=ub[p % 2][0:n, :], scalar=winv[0:n, 1:2], in1=sil[0:n, p % 2, :],
                    op0=ALU.mult, op1=ALU.mult).then_inc(mult_done, 1)

            def hidden_low(i, p):
                n = pair_rows(p)
                dve.wait_ge(hh_done, at_pair(i, p))
                tt(hl[0:n, p % 2, :], h[0:n, p % 2, :], hh[0:n, p % 2, :].bitcast(F32),
                   ALU.subtract).then_inc(hl_done, 1)

            def add_chunk(i, p):
                n, b = pair_rows(p), p // 4 % 2
                if p in (4 * HN, *range(0, 4 * HN, 4)):
                    nc.vector.tensor_copy(acc[0:n, b, :], h[0:n, p % 2, :]).then_inc(acc_done, 1)
                else:
                    dve.wait_ge(acc_done, at_pair(i, p - 1))
                    tt(acc[0:n, b, :], acc[0:n, b, :], h[0:n, p % 2, :], ALU.add).then_inc(acc_done, 1)

            def folded_low(i, n):
                rows = P if n < HN else W2
                dve.wait_ge(hfh_done, i * (HN + 1) + n + 1)
                tt(hf_l[0:rows, n, :], acc[0:rows, n % 2, :], hf_h[0:rows, n, :].bitcast(F32),
                   ALU.subtract).then_inc(hfl_done, 1)

            def z2_stack(i):
                dve.wait_ge(zh2_done, i + 1)
                ts(z2f, zb[0:12, :], 0.5, None, ALU.mult)
                nc.vector.drain()
                stt(out=hf_h[96:108, HN, :], in0=zh2[:].bitcast(F32), scalar=low[0:12, 2:3], in1=z2f,
                    op0=ALU.mult, op1=ALU.add).then_inc(z2_read, 1)

            def aggregate(q):
                nc.vector.tensor_copy(delay[:], i8[:, q, :])
                nc.vector.tensor_copy(wk[:, 0:TOPK], wts[:, q, 0:TOPK])
                nc.vector.memset(agg[:], 0.0)
                nc.vector.drain()
                with dve.Fori(0, TOPK):
                    for b in range(10):
                        ts(bit_i[:, b:b + 1], delay[:, 0:1], b, 1, ALU.logical_shift_right, ALU.bitwise_and)
                    nc.vector.drain()
                    nc.vector.tensor_copy(bit[:], bit_i[:])
                    nc.vector.drain()
                    ts(nbit[:], bit[:], -1.0, 1.0, ALU.mult, ALU.add)
                    nc.vector.drain()
                    src = xn
                    for b in range(10):
                        dst, n, on = rot[b % 2], 1 << b, bit[:, b:b + 1]
                        ts(dst[:], src[:], nbit[:, b:b + 1], None, ALU.mult)
                        nc.vector.drain()
                        stt(out=dst[:, 0:L - n], in0=src[:, n:L], scalar=on, in1=dst[:, 0:L - n],
                            op0=ALU.mult, op1=ALU.add)
                        stt(out=dst[:, L - n:L], in0=src[:, 0:n], scalar=on, in1=dst[:, L - n:L],
                            op0=ALU.mult, op1=ALU.add)
                        nc.vector.drain()
                        src = dst
                    stt(out=agg[:], in0=src[:], scalar=wk[:, 0:1], in1=agg[:], op0=ALU.mult, op1=ALU.add)
                    nc.vector.drain()
                    nc.vector.tensor_copy(dtmp[:, 0:7], delay[:, 1:8])
                    nc.vector.tensor_copy(wtmp[:, 0:TOPK - 1], wk[:, 1:TOPK])
                    nc.vector.drain()
                    nc.vector.tensor_copy(delay[:, 0:7], dtmp[:, 0:7])
                    nc.vector.tensor_copy(wk[:, 0:TOPK - 1], wtmp[:, 0:TOPK - 1])
                    nc.vector.drain()
                nc.vector.tensor_copy(xn[:], agg[:])
                nc.vector.drain()

            def final(i, q, flag):
                buf = xfs[q % 2]
                dve.wait_ge(s_done, at_tile(i, q))
                nc.vector.tensor_copy(c_t[:, 0:1], xn[:, 0:1])
                nc.vector.drain()
                with dve.If(flag > 0):
                    aggregate(q)
                dve.wait_ge(dn_read, at_tile(i, q, 2, 2))
                tt(mir[:], mir[:], xn[:], ALU.mult)
                nc.vector.drain()
                tt(buf[:], buf[:], mir[:], ALU.add).then_inc(final_done, 1)

            def body(i, last):
                current(i)
                for p in range(NP_):
                    if not last and p in STATS_AT:
                        stats(i, STATS_AT.index(p))
                    product(i, p)
                    if p:
                        hidden_low(i, p - 1)
                        add_chunk(i, p - 1)
                    if p - 2 in INV_AT:
                        top(i, INV_AT.index(p - 2))
                    if p == 11:
                        distances()
                    if p == 13:
                        weights(i)
                    if not last and p - 1 in T_AT:
                        folds_low(i, T_AT.index(p - 1))
                    if p % 4 == 2 and p > 2:
                        folded_low(i, p // 4 - 1)
                hidden_low(i, NP_ - 1)
                add_chunk(i, NP_ - 1)
                folded_low(i, HN - 1)
                if not last:
                    quarters_low(i)
                folded_low(i, HN)
                z2_stack(i)
                if not last:
                    z_stack(i)
                dve.wait_ge(rall_done, i + 1)
                ts(some[:], rest_all[:], 0.0, None, ALU.is_gt)
                nc.vector.drain()
                flag = dve.value_load(some[0:1, 0:1])
                for q in range(4):
                    final(i, q, flag)
                if not last:
                    spectrum(i)

            def w_max(m):
                dve.wait_ge(w_loaded[m], 16 if m == 0 else 32)
                for k in range(2):
                    nc.vector.tensor_reduce(wmax[:, m, k:k + 1], raw_w[m][:, k, :], AX_X, ALU.max,
                                            apply_absolute_value=True)
                nc.vector.drain()
                stt(out=wone[:, m:m + 1], in0=wmax[:, m, 0:1], scalar=1e-30, in1=wmax[:, m, 1:2],
                    op0=ALU.max, op1=ALU.max).then_inc(wmax_done, 1)

            def w_scale(m):
                s = slice(m, m + 1)
                dve.wait_ge(wall_done, m + 1)
                ts(wpow[:, s], wall[:, s].bitcast(I32), 0x7F800000, None, ALU.bitwise_and)
                nc.vector.drain()
                ts(winv[:, s], wpow[:, s].bitcast(F32), 2.0 ** -14, None, ALU.mult)
                nc.vector.drain()
                nc.vector.reciprocal(wscl[:, s], winv[:, s])
                nc.vector.drain()
                ts(bscl[:, s], wscl[:, s], 0.5, None, ALU.mult).then_inc(wscl_done, 1)

            def w_low(m):
                for k in range(2):
                    dve.wait_ge(wh_done, 2 * m + k + 1)
                    stt(out=wt_l[m][:, k, :], in0=raw_w[m][:, k, :], scalar=wscl[:, m:m + 1],
                        in1=wt_h[m][:, k, :], op0=ALU.mult, op1=ALU.subtract).then_inc(wl_done, 1)

            stats(-1, 0)
            dve.wait_ge(folded, 1)
            ts(xqf[0:4, :], xqf[0:4, :], 0.25, None, ALU.mult)
            nc.vector.drain()
            ts(xqf[0:4, 0:512:256], xqf[0:4, 0:512:256], 2.0, None, ALU.mult)
            ts(xqf[0:4, 767:1024:256], xqf[0:4, 767:1024:256], 2.0, None, ALU.mult).then_inc(small_done, 1)
            stats(-1, 1)
            dve.wait_ge(m_ready, 1)
            m0 = mb[0][:, 0:32]
            nc.vector.tensor_copy(a_bf[:, 0, :], m0)
            nc.vector.drain()
            tt(a_r[:, 0, :], m0, a_bf[:, 0, :], ALU.subtract).then_inc(m_free, 1)
            nc.vector.drain()
            nc.vector.tensor_copy(a_bf[:, 1, :], a_r[:, 0, :])
            nc.vector.drain()
            tt(a_r[:, 1, :], a_r[:, 0, :], a_bf[:, 1, :], ALU.subtract)
            nc.vector.drain()
            nc.vector.tensor_copy(a_bf[:, 2, :], a_r[:, 1, :])
            nc.vector.drain()
            w_max(0)
            w_scale(0)
            stats(-1, 2)
            w_low(0)
            folds_low(-1, 0)
            w_max(1)
            folds_low(-1, 1)
            w_scale(1)
            stats(-1, 3)
            nc.vector.drain()
            for m in range(2):
                o = ts(raw_b[:, :, m, :], raw_b[:, :, m, :], bscl[:, m:m + 1], None, ALU.mult)
            o.then_inc(b_sc_done, 1)
            w_low(1)
            folds_low(-1, 2)
            dve.wait_ge(b_hi_done, 1)
            dve.wait_ge(stored, 16)
            stt(out=bst[:], in0=b_hi[:].bitcast(F32), scalar=low[:, 1:2], in1=raw_b[:], op0=ALU.mult, op1=ALU.add)
            nc.vector.drain()
            for q in range(4):
                nc.vector.memset(zst[q][:].bitcast(F32), 0.0)
            dve.wait_ge(zeroed, 1)
            for u in range(7):
                for q in range(4):
                    o = nc.vector.tensor_copy(ast[:, :, 32 * q + 4 * u:32 * q + 4 * u + 4],
                                              a_bf[:, u // 3, :].rearrange("p (k r) -> p k r", k=8))
            o.then_inc(small_done, 1)
            folds_low(-1, 3)
            quarters_low(-1)
            dve.wait_ge(a2h_done, 1)
            tt(a2_l[:], raw_a2[:], a2_h[:].bitcast(F32), ALU.subtract)
            nc.vector.drain()
            for u in range(6):
                o = nc.vector.tensor_copy(a2st[:, :, 2 * u:2 * u + 2], (a2_h if u < 3 else a2_l)[:].bitcast(F32))
            o.then_inc(small_done, 1)
            z_stack(-1)
            for n in range(HN + 1):
                dve.wait_ge(w2h_done, n + 1)
                rows = P if n < HN else 96
                tt(w2_l[0:rows, n, :], raw_w2[0:rows, n, :], w2_h[0:rows, n, :].bitcast(F32), ALU.subtract)
            nc.vector.memset(w2_l[96:P, HN, :].bitcast(F32), 0.0)
            stt(out=w2_h[96:P, HN, :], in0=w2_h[96:P, HN, :].bitcast(F32), scalar=low[96:P, 3:4],
                in1=raw_w2[96:P, HN, :], op0=ALU.mult, op1=ALU.add).then_inc(w2l_done, 1)
            nc.vector.drain()
            nc.vector.memset(hf_h[96:P, HN, :].bitcast(F32), 0.0)
            nc.vector.memset(hf_l[96:P, HN, :].bitcast(F32), 0.0).then_inc(z2_read, 1)
            nc.vector.drain()
            spectrum(-1)
            with dve.Fori(0, NG - 1) as i:
                body(i, False)
            body(NG - 1, True)

        @block.tensor
        def _(pe):
            mm = nc.tensor.matmul

            def chain(out, terms):
                for n, (a, b) in enumerate(terms):
                    o = mm(out, a, b, start=n == 0, stop=n == len(terms) - 1)
                return o

            def three(a, b):
                return [(a[0], b[0]), (a[0], b[1]), (a[1], b[0])]

            def bank_free(i, k):
                if 3 <= k < 3 + 4:
                    if not (isinstance(i, int) and i < 0):
                        pe.wait_ge(inv_read, at_tile(i, k - 3))
                    elif k == 6:
                        pe.wait_ge(m_free, at_free(i, 3))
                elif k >= 7:
                    pe.wait_ge(m_free, at_free(i, k - 3))
                else:
                    pe.wait_ge(m_free, at_free(i - 1, k + 12))

            def folds_across(i, q):
                pe.wait_ge(folded, (i + 1) * 4 + q + 2)
                for k in range(2):
                    use = USE_T + 2 * q + k
                    bank_free(i, use)
                    for j in range(4):
                        c = (4 * k + j) * P
                        o = nc.tensor.transpose(mb[use % 3][:, j * P:(j + 1) * P], xfs[q % 2][:, c:c + P], ident[:])
                    o.then_inc(m_ready, 1)

            def quarters_across(i):
                pe.wait_ge(quartered, (i + 2) * 12)
                for k in range(2):
                    bank_free(i, USE_XFT + k)
                    for q in range(4):
                        o = nc.tensor.transpose(mb[(USE_XFT + k) % 3][:, q * P:(q + 1) * P],
                                                xq[:, q, k * P:(k + 1) * P], ident[:])
                    o.then_inc(m_ready, 1)

            def rank_in(i):
                bank_free(i, USE_XA)
                pe.wait_ge(m_free, at_free(i, USE_T + 7))
                chain(mb[USE_XA % 3][:], [(ast[:, k, :], f[:, k, :]) for k in range(8) for f in (ft_h, ft_l)])\
                    .then_inc(m_ready, 1)

            def dft(i):
                for dd in range(4):
                    s = NP_ + 4 + dd
                    c = slice(P * (dd % 2), P * (dd % 2) + P)
                    cos_k, sin_k = ((0, 1), (6, 7)) if dd < 2 else ((2, 3), (4, 5))
                    for bank, ks, ready, n in ((gb[s % 2], cos_k, g_ready, 1), (ub[s % 2], sin_k, u_ready, 2)):
                        if dd >= 2:
                            pe.wait_ge(sq_done, at_tile(i + 1, dd - 2, 2, n))
                        elif not (isinstance(i, int) and i < 0):
                            pe.wait_ge(dn_read, at_tile(i, dd + 2, 2, n))
                        terms = [t for k in ks for t in three((fwd_h[:, k, c], fwd_l[:, k, c]),
                                                              (ft_h[:, k, :], ft_l[:, k, :]))]
                        if ks == (0, 1):
                            terms += [(mid[:, c], ft_h[:, 7, :]), (mid[:, c], ft_l[:, 7, :])]
                        chain(bank[:], terms).then_inc(ready, 1)

            def inverse(i, q):
                if q == 0:
                    pe.wait_ge(ql_done, (i + 1) * 4)
                bank_free(i, q)
                t = slice(q * P, (q + 1) * P)
                for odd in range(2):
                    o = chain(mb[q % 3][:, 256 * odd:256 * odd + 256],
                              [x for k in (2 * odd, 2 * odd + 1)
                               for x in three((qt_h[:, k, t], qt_l[:, k, t]), (inv_h[:, k, :], inv_l[:, k, :]))])
                o.then_inc(m_ready, 1)

            def up(i, p):
                n, c, b = pair_rows(p), pair_col(p), p % 2
                for m, (bank, ready) in enumerate(((gb[b], g_ready), (ub[b], u_ready))):
                    if p < 2:
                        pe.wait_ge(sq_done, at_tile(i, p + 2, 2, m + 1))
                    elif m == 0:
                        pe.wait_ge(sil_done, at_pair(i, p - 2))
                    else:
                        pe.wait_ge(mult_done, at_pair(i, p - 2))
                    terms = [t for k in range(2) for t in three((wt_h[m][:, k, c:c + n], wt_l[m][:, k, c:c + n]),
                                                                (xt_h[:, k, :], xt_l[:, k, :]))]
                    terms.append((bst[:, p // 4, m, 0:n], zst[p % 4][:]))
                    chain(bank[0:n, :], terms).then_inc(ready, 1)

            def z2(i, p):
                n = pair_rows(p)
                if p == 0:
                    pe.wait_ge(z2_read, i + 1)
                pe.wait_ge(hh_done, at_pair(i, p))
                mm(zb[0:12, :], a2st[0:n, p, :], hh[0:n, p % 2, :], start=p == 0, stop=False)
                pe.wait_ge(hl_done, at_pair(i, p))
                mm(zb[0:12, :], a2st[0:n, p, :], hl[0:n, p % 2, :], start=False,
                   stop=p == NP_ - 1).then_inc(z2_done, 1)

            def down(i, q):
                if q == 0:
                    pe.wait_ge(w2l_done, 1)
                s, t = NP_ + q, slice(q * P, (q + 1) * P)
                banks = ((gb[s % 2], 0), (ub[s % 2], 512))
                if q < 2:
                    pe.wait_ge(sil_done, at_pair(i, NP_ - 2 + q))
                    pe.wait_ge(mult_done, at_pair(i, NP_ - 2 + q))
                else:
                    pe.wait_ge(dn_read, at_tile(i, q - 2, 2, 2))
                for n in range(HN + 1):
                    if q == 0:
                        pe.wait_ge(hfl_done, i * (HN + 1) + n + 1)
                        if n == HN:
                            pe.wait_ge(z2_read, i + 2)
                    last = n == HN
                    for bank, c in banks:
                        mm(bank[:], hf_h[:, n, t], w2_h[:, n, c:c + 512], start=n == 0, stop=False)
                    for bank, c in banks:
                        mm(bank[:], hf_h[:, n, t], w2_l[:, n, c:c + 512], start=False, stop=False)
                    for (bank, c), ready in zip(banks, (g_ready, u_ready)):
                        o = mm(bank[:], hf_l[:, n, t], w2_h[:, n, c:c + 512], start=False, stop=last)
                        if last:
                            o.then_inc(ready, 1)

            def body(i, last):
                for p in range(NP_):
                    up(i, p)
                    if p >= 2:
                        z2(i, p - 2)
                    if p in INV_AT:
                        inverse(i, INV_AT.index(p))
                    if not last and p in T_AT:
                        folds_across(i, T_AT.index(p))
                z2(i, NP_ - 2)
                if not last:
                    quarters_across(i)
                z2(i, NP_ - 1)
                if not last:
                    rank_in(i)
                for q in range(4):
                    down(i, q)
                if not last:
                    dft(i)

            pe.wait_ge(a_loaded, 32)
            pe.wait_ge(small_done, 1)
            for k in range(8):
                o = nc.tensor.transpose(mb[0][:, 4 * k:4 * k + 4], xqf[0:4, k * P:(k + 1) * P], ident[0:4, 0:4])
            o.then_inc(m_ready, 1)
            for q in range(4):
                folds_across(-1, q)
            quarters_across(-1)
            pe.wait_ge(small_done, 2)
            rank_in(-1)
            pe.wait_ge(c_loaded, 16 * N_CONST)
            dft(-1)
            pe.wait_ge(m_free, at_free(-1, USE_XA))
            pe.wait_ge(wl_done, 4)
            pe.wait_ge(small_done, 3)
            with pe.Fori(0, NG - 1) as i:
                body(i, False)
            body(NG - 1, True)


def kernel(**inputs):
    import concourse.bacc as _bacc
    from concourse.bass_utils import run_bass_kernel_spmd as _run

    g = {k.replace("L0_ffn_", "").replace("L0_attn_", ""): np.ascontiguousarray(v) for k, v in inputs.items()}
    order = hidden_order()

    def transposed(w):
        return np.ascontiguousarray(w[order].T.reshape(2, P, HID).transpose(1, 0, 2))

    def by_pair(rows):
        out = np.zeros((NP_, P, rows.shape[0]), rows.dtype)
        for p in range(NP_):
            c, n = pair_col(p), pair_rows(p)
            out[p, :n] = rows[:, order[c:c + n]].T
        return out

    b13 = np.zeros((P, 6, 2, P), g["b1"].dtype)
    for m, b in enumerate((g["b1"], g["b3"])):
        bp = by_pair(np.ascontiguousarray(b.T))
        for p in range(NP_):
            for u in range(7):
                r0 = 32 * (p % 4) + 4 * u + 2 * m
                b13[r0:r0 + 2, p // 4, m, :] = bp[p].T
    w2t = np.zeros((P, HN + 1, L), g["w2q"].dtype)
    for n in range(HN):
        w2t[:, n] = g["w2q"][:, n * P:(n + 1) * P].T
    w2t[0:TAIL, HN] = w2t[TAIL:W2, HN] = g["w2q"][:, HN * P:].T
    for u in range(6):
        w2t[96 + 2 * u:98 + 2 * u, HN] = g["b2"].T
    arrays = dict(
        x=g["x"].reshape(TOK, L), w1t=transposed(g["w1q"]), w3t=transposed(g["w3q"]),
        a13=np.concatenate([g["a1"], g["a3"]]), b13=b13, w2t=w2t,
        a2t=np.ascontiguousarray(by_pair(g["a2"]).transpose(1, 0, 2)), **constants())

    nc = _bacc.Bacc("TRN2", target_bir_lowering=False, num_devices=1, dynamic_dma_scratch_size=1024)
    dram = {k: nc.dram_tensor(f"in_{k}", v.shape, mybir.dt.from_np(v.dtype), kind="ExternalInput").ap()
            for k, v in arrays.items()}
    dram["out"] = nc.dram_tensor("out_x", (TOK, L), F32, kind="ExternalOutput").ap()
    build(nc, dram)
    r = _run(nc, [{f"in_{k}": v for k, v in arrays.items()}], core_ids=[0])
    return r.results[0]["out_x"].reshape(g["x"].shape)
```
